# Optimizing a Trainium2 kernel written in Bass

```python
import numpy as np
import jax
import jax.numpy as jnp

def _softmax(x, axis=-1):
    return jax.nn.softmax(x, axis=axis)

def _gelu(x):
    return jax.nn.gelu(x, approximate=True)

def _silu(x):
    return jax.nn.silu(x)

def _sigmoid(x):
    return jax.nn.sigmoid(x)

def _layernorm(x, axis=-1, eps=1e-05):
    m = jnp.mean(x, axis=axis, keepdims=True)
    v = jnp.var(x, axis=axis, keepdims=True)
    return (x - m) / jnp.sqrt(v + eps)

def _scatter_add(tgt, idx, src, axis=0):
    return tgt.at[idx].add(src)

def _segment_sum(src, seg, n):
    return jax.ops.segment_sum(src, seg, n)
kernel_name = 'mk_dlrm_tower_d1_rec_r8_c92540'

def setup_inputs(seed: int=0):
    np.random.seed(seed)
    _w = jnp.asarray

    def _rec_inputs():
        import jax
        import jax.numpy as jnp
        _tk = jax.random.key(seed)
        dense_ctx = jax.random.normal(jax.random.fold_in(_tk, 190), (1024, 16), jnp.float32)
        ids = jnp.stack([jax.random.randint(jax.random.fold_in(_tk, 200 + f), (1024,), 0, v, jnp.int32) for f, v in enumerate([12500, 12500, 1000, 1000, 1000, 1250, 1000, 1000])], axis=1)
        tbl_0 = 0.05 * jax.random.normal(jax.random.fold_in(_tk, 500 + 0), (12500, 1024), jnp.float32)
        tbl_1 = 0.05 * jax.random.normal(jax.random.fold_in(_tk, 500 + 1), (12500, 1024), jnp.float32)
        tbl_2 = 0.05 * jax.random.normal(jax.random.fold_in(_tk, 500 + 2), (1000, 1024), jnp.float32)
        tbl_3 = 0.05 * jax.random.normal(jax.random.fold_in(_tk, 500 + 3), (1000, 1024), jnp.float32)
        tbl_4 = 0.05 * jax.random.normal(jax.random.fold_in(_tk, 500 + 4), (1000, 1024), jnp.float32)
        tbl_5 = 0.05 * jax.random.normal(jax.random.fold_in(_tk, 500 + 5), (1250, 1024), jnp.float32)
        tbl_6 = 0.05 * jax.random.normal(jax.random.fold_in(_tk, 500 + 6), (1000, 1024), jnp.float32)
        tbl_7 = 0.05 * jax.random.normal(jax.random.fold_in(_tk, 500 + 7), (1000, 1024), jnp.float32)
        _rk = jax.random.fold_in(_tk, 7)
        W_top1 = 0.0310087 * jax.random.normal(jax.random.fold_in(_tk, 801), (1040, 512), jnp.float32)
        W_top2 = 0.0441942 * jax.random.normal(jax.random.fold_in(_tk, 802), (512, 256), jnp.float32)
        W_top3 = 0.0625 * jax.random.normal(jax.random.fold_in(_tk, 803), (256, 1), jnp.float32)
        b_top1 = jnp.zeros((512,), jnp.float32)
        b_top2 = jnp.zeros((256,), jnp.float32)
        return (dense_ctx, ids, tbl_0, tbl_1, tbl_2, tbl_3, tbl_4, tbl_5, tbl_6, tbl_7, W_top1, b_top1, W_top2, b_top2, W_top3)
    dense_ctx, ids, tbl_0, tbl_1, tbl_2, tbl_3, tbl_4, tbl_5, tbl_6, tbl_7, W_top1, b_top1, W_top2, b_top2, W_top3 = _rec_inputs()

    def _L0_rec_setup():
        import jax, jax.numpy as jnp
        import numpy as np
        B, F, H = (1024, 8, 1024)

        def _linear_params(key, fan_in, fan_out):
            kw, kb = jax.random.split(key)
            w = jax.random.normal(kw, (fan_in, fan_out), dtype=jnp.float32) * 0.02
            b = jax.random.normal(kb, (fan_out,), dtype=jnp.float32) * 0.02
            return (w, b)
        key = jax.random.key(seed)
        ks = jax.random.split(key, 7)
        field_vectors = jax.random.normal(ks[0], (B, F, H), dtype=jnp.float32)
        Wn1, bn1 = _linear_params(ks[1], H, H)
        Wn2, bn2 = _linear_params(ks[2], H, H)
        Wa1, ba1 = _linear_params(ks[3], 2 * H, H)
        Wa2, ba2 = _linear_params(ks[4], H, H)
        Wo1, bo1 = _linear_params(ks[5], 2 * H, H)
        Wo2, bo2 = _linear_params(ks[6], H, H)
        not_idx = jnp.array([2, 3], dtype=jnp.int64)
        and_pairs = jnp.array([[0, 1], [2, 3]], dtype=jnp.int64)
        or_pairs = jnp.array([[4, 5]], dtype=jnp.int64)
        return {'field_vectors': field_vectors, 'Wn1': Wn1, 'bn1': bn1, 'Wn2': Wn2, 'bn2': bn2, 'Wa1': Wa1, 'ba1': ba1, 'Wa2': Wa2, 'ba2': ba2, 'Wo1': Wo1, 'bo1': bo1, 'Wo2': Wo2, 'bo2': bo2, 'not_idx': not_idx, 'and_pairs': and_pairs, 'or_pairs': or_pairs}
    _L0_rec_all = _L0_rec_setup()
    _L0_rec_in = {k: v for k, v in _L0_rec_all.items() if k in ('Wn1', 'bn1', 'Wn2', 'bn2', 'Wa1', 'ba1', 'Wa2', 'ba2', 'Wo1', 'bo1', 'Wo2', 'bo2', 'not_idx', 'and_pairs', 'or_pairs')}
    del _L0_rec_all
    return {'dense_ctx': dense_ctx, 'ids': ids, 'tbl_0': tbl_0, 'tbl_1': tbl_1, 'tbl_2': tbl_2, 'tbl_3': tbl_3, 'tbl_4': tbl_4, 'tbl_5': tbl_5, 'tbl_6': tbl_6, 'tbl_7': tbl_7, 'W_top1': W_top1, 'b_top1': b_top1, 'W_top2': W_top2, 'b_top2': b_top2, 'W_top3': W_top3, 'L0_rec_Wn1': _L0_rec_in['Wn1'], 'L0_rec_bn1': _L0_rec_in['bn1'], 'L0_rec_Wn2': _L0_rec_in['Wn2'], 'L0_rec_bn2': _L0_rec_in['bn2'], 'L0_rec_Wa1': _L0_rec_in['Wa1'], 'L0_rec_ba1': _L0_rec_in['ba1'], 'L0_rec_Wa2': _L0_rec_in['Wa2'], 'L0_rec_ba2': _L0_rec_in['ba2'], 'L0_rec_Wo1': _L0_rec_in['Wo1'], 'L0_rec_bo1': _L0_rec_in['bo1'], 'L0_rec_Wo2': _L0_rec_in['Wo2'], 'L0_rec_bo2': _L0_rec_in['bo2'], 'L0_rec_not_idx': _L0_rec_in['not_idx'], 'L0_rec_and_pairs': _L0_rec_in['and_pairs'], 'L0_rec_or_pairs': _L0_rec_in['or_pairs']}

def reference(dense_ctx, ids, tbl_0, tbl_1, tbl_2, tbl_3, tbl_4, tbl_5, tbl_6, tbl_7, W_top1, b_top1, W_top2, b_top2, W_top3, L0_rec_Wn1, L0_rec_bn1, L0_rec_Wn2, L0_rec_bn2, L0_rec_Wa1, L0_rec_ba1, L0_rec_Wa2, L0_rec_ba2, L0_rec_Wo1, L0_rec_bo1, L0_rec_Wo2, L0_rec_bo2, L0_rec_not_idx, L0_rec_and_pairs, L0_rec_or_pairs):
    import jax
    import jax.numpy as jnp

    def _L0_rec_ref(field_vectors, Wn1, bn1, Wn2, bn2, Wa1, ba1, Wa2, ba2, Wo1, bo1, Wo2, bo2, not_idx, and_pairs, or_pairs):
        import jax, jax.numpy as jnp
        import numpy as np
        B, F, H = (1024, 8, 1024)

        def _linear_params(key, fan_in, fan_out):
            kw, kb = jax.random.split(key)
            w = jax.random.normal(kw, (fan_in, fan_out), dtype=jnp.float32) * 0.02
            b = jax.random.normal(kb, (fan_out,), dtype=jnp.float32) * 0.02
            return (w, b)
        num_fields = field_vectors.shape[1]
        x_not = jnp.take(field_vectors, not_idx, axis=1)
        t = jnp.tanh(jax.nn.relu(x_not @ Wn1 + bn1) @ Wn2 + bn2)
        iv = field_vectors.at[:, not_idx, :].set(t)

        def pair_fuse(pairs, W1, b1, W2, b2):
            v = jnp.concatenate([jnp.take(iv, pairs[:, 0], axis=1), jnp.take(iv, pairs[:, 1], axis=1)], axis=-1)
            return jax.nn.relu(v @ W1 + b1) @ W2 + b2
        and_out = pair_fuse(and_pairs, Wa1, ba1, Wa2, ba2)
        or_out = pair_fuse(or_pairs, Wo1, bo1, Wo2, bo2)
        processed = jnp.zeros((num_fields,), dtype=field_vectors.dtype).at[and_pairs.reshape(-1)].set(1.0).at[or_pairs.reshape(-1)].set(1.0)
        remaining = 1.0 - processed
        sum_res = and_out.sum(axis=1) + or_out.sum(axis=1) + jnp.einsum('bfh,f->bh', iv, remaining)
        count = and_pairs.shape[0] + or_pairs.shape[0] + remaining.sum()
        return sum_res / count
    e = jnp.stack([tbl_0[ids[:, 0]], tbl_1[ids[:, 1]], tbl_2[ids[:, 2]], tbl_3[ids[:, 3]], tbl_4[ids[:, 4]], tbl_5[ids[:, 5]], tbl_6[ids[:, 6]], tbl_7[ids[:, 7]]], axis=1)
    z = _L0_rec_ref(e, L0_rec_Wn1, L0_rec_bn1, L0_rec_Wn2, L0_rec_bn2, L0_rec_Wa1, L0_rec_ba1, L0_rec_Wa2, L0_rec_ba2, L0_rec_Wo1, L0_rec_bo1, L0_rec_Wo2, L0_rec_bo2, L0_rec_not_idx, L0_rec_and_pairs, L0_rec_or_pairs)
    z = z.reshape(z.shape[0], -1)
    h = jnp.concatenate([z, dense_ctx], axis=1)
    h = jnp.maximum(h @ W_top1 + b_top1, 0.0)
    h = jnp.maximum(h @ W_top2 + b_top2, 0.0)
    y = h @ W_top3
    return y

_drawn_inputs = setup_inputs


def setup_inputs(seed=0):
    import zlib

    import numpy as np

    out = dict(_drawn_inputs(seed))
    spreads = {'b_top1': (0.0, 0.1), 'b_top2': (0.0, 0.1)}
    factors = {'tbl_0': 4.254,
     'tbl_1': 4.286,
     'tbl_2': 8.0,
     'tbl_3': 8.0,
     'tbl_4': 4.657,
     'tbl_5': 4.544,
     'L0_rec_Wn1': 8.0,
     'L0_rec_bn1': 8.0,
     'L0_rec_Wn2': 8.0,
     'L0_rec_bn2': 8.0,
     'L0_rec_Wa1': 2.915,
     'L0_rec_ba1': 3.999,
     'L0_rec_Wo1': 3.447,
     'L0_rec_bo1': 8.0,
     'L0_rec_Wo2': 2.872}
    for name, (base, spread) in spreads.items():
        noise = np.random.default_rng([zlib.crc32(name.encode()), seed]).standard_normal(out[name].shape)
        drawn = base * np.exp(spread * noise) if base else spread * noise
        out[name] = jnp.asarray(drawn.astype(out[name].dtype))
    for name, factor in factors.items():
        out[name] = (out[name] * factor).astype(out[name].dtype)
    return out
```

```python
from contextlib import ExitStack

import numpy as np

import concourse.bass as bass
from concourse import mybir

F32 = mybir.dt.float32
F32R = mybir.dt.float32r
I32 = mybir.dt.int32
ACT = mybir.ActivationFunctionType
ALU = mybir.AluOpType
AX = mybir.AxisListType

P = 128
Q = 4
LANE = 32
B, F, H = 1024, 8, 1024
D = 16
M1, M2 = 512, 256
VOCAB = [12500, 12500, 1000, 1000, 1000, 1250, 1000, 1000]
KT = H // P
HALVES = 2
HALF = B // HALVES
GATHERS = HALF // LANE
QUARTER = H // Q
NPAIR = 3
SLOTS = 2 + 2 * NPAIR
SPARE = F - SLOTS + 2
N0, N1, A00, A01, A10, A11, O0, O1 = range(SLOTS)
REST = SLOTS

TILES_N = 2 * KT
TILES_A = 2 * KT
TILES_O = 4 * KT
TILES_MID = 2 * TILES_N + 2 * TILES_A + TILES_O
TILES_T1 = KT
TILES_T2 = M1 // P
TILES = TILES_MID + TILES_T1 + TILES_T2
STAGE = 4
RING = 2
BANKS = 8
EVEN = BANKS // 2
GROUPS = 8
DONE_GROUP = BANKS - 1
DONE_TOP = GROUPS * DONE_GROUP
DONE_HALF = DONE_TOP + 3 + 1 + 2
FREED_HALF = (GROUPS + 1) * EVEN
GSTAGE = 8

REST_JOB = "rest"
JOBS = [N1, A00, A01, A10, REST_JOB, A11, O0, O1, N0]
UNITS_AHEAD = GATHERS
FIRST_UNIT = {job: UNITS_AHEAD + GATHERS * (i + (i > JOBS.index(REST_JOB))) for i, job in enumerate(JOBS)}
UNITS_HALF = GATHERS * (len(JOBS) + 1)

BN1, BN2, BA1, BA2, BO1, BO2, BT1 = (KT * i for i in range(7))
BT2 = BT1 + M1 // P
W3C = BT2 + M2 // P
NBIAS = W3C + M2 // P
C_FIELD, C_BASE, C_RANK, C_OWN, C_TO0, C_TO1 = (F * i for i in range(6))
C_UPTO = 6 * F
NCONST = C_UPTO + F * F
E0, T0, HID, HSUM, Z, ENTRIES = 0, 4, 6, 7, 8, 9
ENTRY = KT * HALF
ENTRY_OF = {slot: E0 + slot % 4 for slot in range(SLOTS)}


def build_tower(nc, table, ids, fields, consts, biases, w_mid, w_t1, w_t2, w_dense, dense, out):
    with ExitStack() as ctx:
        def sb(name, shape, dt=F32):
            return ctx.enter_context(nc.sbuf_tensor(name, shape, dt))

        def sem(name):
            return ctx.enter_context(nc.semaphore(name))

        acts = sb("acts", [P, ENTRIES, KT, HALF])
        acts_flat = acts[:].rearrange("p e k n -> p (e k n)")

        w_raw = sb("w_raw", [P, STAGE, H])
        w_hl = sb("w_hl", [P, RING, 2, H], F32R)
        x_hl = sb("x_hl", [P, RING, 2, HALF], F32R)
        rows = sb("rows", [P, GSTAGE, QUARTER])
        rest_sum = sb("rest_sum", [P, QUARTER])
        more_rows = sb("more_rows", [P, QUARTER])
        more_turned = sb("more_turned", [P, KT, LANE])
        more_idx = sb("more_idx", [P, 1], I32)
        idx = sb("idx", [P, HALVES, SLOTS + F, GATHERS], I32)
        dense_sb = sb("dense_sb", [D, HALF])
        w_dense_sb = sb("w_dense_sb", [D, M1])
        bias = sb("bias", [P, NBIAS])
        const = sb("const", [P, NCONST])
        field_i = sb("field_i", [P, F], I32)
        field_f = sb("field_f", [P, F])
        onehot = sb("onehot", [P, SLOTS + F, F])
        mask = sb("mask", [P, 5, F])
        square = sb("square", [P, F, F])
        scal = sb("scal", [P, 16])
        left_over = sb("left_over", [P, F])
        same = sb("same", [P, 4, 2 * NPAIR])
        sel_f = sb("sel_f", [P, 2 * NPAIR + 1])
        sel_i = sb("sel_i", [P, 2 * NPAIR + 1], I32)
        bias_z = sb("bias_z", [P, KT])
        y_sb = sb("y_sb", [1, HALF])
        warm = sb("warm", [1, 1])
        ids_i = more_rows[:].bitcast(I32)
        row_f = rest_sum[:]
        picked = sb("picked", [P, GATHERS * HALVES, F])

        psum = ctx.enter_context(nc.psum_tensor("psum", [P, BANKS, HALF], F32))

        consts_in = sem("consts_in")
        top_in = sem("top_in")
        w_staged = [sem(f"w_staged{i}") for i in range(STAGE)]
        setup = sem("setup")
        sources_done = sem("sources_done")
        idx_done = sem("idx_done")
        gathered = [sem(f"gathered{i}") for i in range(GSTAGE)]
        turned = sem("turned")
        rest_turned = sem("rest_turned")
        w_hi = sem("w_hi")
        w_lo = sem("w_lo")
        x_hi = sem("x_hi")
        x_lo = sem("x_lo")
        tile_done = sem("tile_done")
        bank_done = sem("bank_done")
        freed_act = sem("freed_act")
        freed_dve = sem("freed_dve")
        tanh_done = sem("tanh_done")
        pair_added = sem("pair_added")
        z_added = sem("z_added")
        z_ready = sem("z_ready")
        more_asked = sem("more_asked")
        more_seen = sem("more_seen")
        more_got = sem("more_got")
        more_step = sem("more_step")
        stored = sem("stored")

        def x_source(g, k, bases):
            fixed = {0: E0, 1: HID, 2: E0 + 1, 3: HID, 10: HSUM, 11: HID, 12: Z, 13: HID}
            if g in fixed:
                return acts[:, fixed[g], k, :]
            return acts_flat[:, bass.ds(bases[g - 4] + k * HALF, HALF)]

        def slot_turned(h, slot):
            done = UNITS_AHEAD if slot == N0 else FIRST_UNIT[slot] + GATHERS
            return h * UNITS_HALF + GSTAGE + done

        FINISH = {0: "n1", 1: "n2", 2: "n1", 3: "n2", 5: "and0", 7: "and1", 9: "or", 11: "z"}
        INDEX = {g: i for i, g in enumerate(FINISH)}

        def wait_finished(eng, h, g, m):
            if m == BANKS - 1:
                eng.wait_ge(tile_done, h * TILES + RING + (g + 1) * KT)
            else:
                eng.wait_ge(bank_done, h * DONE_HALF + INDEX[g] * DONE_GROUP + m + 1)

        def wait_source(eng, h, g, k):
            freed = h * FREED_HALF + EVEN
            if g in (0, 2, 4, 5, 6, 7, 8, 9):
                slot = {0: N0, 2: N1}.get(g, g - 2)
                if k == 0:
                    eng.wait_ge(turned, slot_turned(h, slot))
            if 4 <= g <= 9:
                if g == 4:
                    eng.wait_ge(freed_act, freed + EVEN * INDEX[3] + (1 if k == 0 else EVEN))
                    if k:
                        eng.wait_ge(tanh_done, h * KT + EVEN + k // 2 + k % 2)
                elif k == 0:
                    eng.wait_ge(tanh_done, h * KT + 2 * EVEN)
            elif g in (1, 3, 11):
                done = freed + EVEN * INDEX[{1: 0, 3: 2, 11: 9}[g]] + k // 2 + 1
                eng.wait_ge(freed_dve if k % 2 else freed_act, done)
            elif g == 10:
                eng.wait_ge(pair_added, (h + 1) * KT)
            elif g == 12:
                eng.wait_ge(z_ready, h * KT + k + 1)
            elif g == 13:
                eng.wait_ge(freed_dve if k % 2 else freed_act, freed + EVEN * GROUPS + k // 2 + 1)

        block = ctx.enter_context(nc.Block())

        @block.sync
        def _(sp):
            sp.dma_start(field_i[:], fields).then_inc(consts_in, 16)
            sp.dma_start(const[:], consts).then_inc(consts_in, 16)
            sp.dma_start(ids_i, ids).then_inc(consts_in, 16)
            sp.dma_start(bias[:], biases).then_inc(consts_in, 16)

            def stream(source, width, first, count, tile):
                def four(i):
                    for s in range(STAGE):
                        sp.wait_ge(w_lo, tile + i * STAGE + s + 1)
                        src = source[bass.ds(first + i * STAGE + s, 1), :, :].rearrange("a p n -> (a p) n")
                        sp.dma_start(w_raw[:, s, 0:width], src).then_inc(w_staged[s], 16)
                if count == STAGE:
                    four(0)
                else:
                    with sp.Fori(0, count // STAGE) as i:
                        four(i)

            with sp.Fori(0, HALVES) as h:
                with sp.Fori(0, 2) as f:
                    stream(w_mid, H, 0, TILES_N, h * TILES + f * TILES_N)
                with sp.Fori(0, 2) as p:
                    stream(w_mid, H, TILES_N, TILES_A, h * TILES + 2 * TILES_N + p * TILES_A)
                stream(w_mid, H, TILES_N + TILES_A, TILES_O, h * TILES + 2 * TILES_N + 2 * TILES_A)
                stream(w_t1, M1, 0, TILES_T1, h * TILES + TILES_MID)
                stream(w_t2, M2, 0, TILES_T2, h * TILES + TILES_MID + TILES_T1)

        @block.gpsimd
        def _(pool):
            def gather(unit, h, column, g):
                pool.wait_ge(turned, unit + 1)
                nc.gpsimd.indirect_dma_start(rows[:, unit % GSTAGE, :], None, table,
                                             bass.IndirectOffsetOnAxis(idx[:, h, column, g:g + 1], 0)
                                             ).then_inc(gathered[unit % GSTAGE], 16)

            def more_gathers(h):
                with pool.Fori(0, GATHERS * (F - 2)) as n:
                    pool.wait_ge(more_asked, h * GATHERS * (F - 2) + n + 1)
                    pool.sem_inc(more_seen, 1)
                    nc.gpsimd.indirect_dma_start(more_rows[:], None, table,
                                                 bass.IndirectOffsetOnAxis(more_idx[:], 0)
                                                 ).then_inc(more_got, 16)

            pool.wait_ge(idx_done, 1)
            for g in range(GATHERS):
                gather(g, 0, N0, g)
            for h in range(HALVES):
                for job in JOBS:
                    unit = h * UNITS_HALF + FIRST_UNIT[job]
                    if job == REST_JOB:
                        pool.wait_ge(idx_done, REST + 2)
                        for g in range(GATHERS):
                            for r in range(2):
                                gather(unit + 2 * g + r, h, REST + r, g)
                        pool.wait_ge(idx_done, REST + F)
                        more = nc.gpsimd.value_load(sel_i[0:1, 2 * NPAIR:2 * NPAIR + 1], min_val=0, max_val=F)
                        with pool.If(more > 2):
                            more_gathers(h)
                    elif job != N0 or h + 1 < HALVES:
                        half = h + (job == N0)
                        pool.wait_ge(idx_done, job + 1)
                        for g in range(GATHERS):
                            gather(unit + g, half, job, g)

        @block.tensor
        def _(pe):
            def three(bank, s, col, start, stop):
                for n, (w, v) in enumerate(((1, 0), (0, 1), (0, 0))):
                    mm = nc.tensor.matmul(psum[:, bank, :], w_hl[:, s, w, col * P:(col + 1) * P],
                                          x_hl[:, s, v, :], start=start and n == 0, stop=stop and n == 2)
                return mm

            def wait_tile(tile):
                pe.wait_ge(w_lo, STAGE + tile + 1)
                pe.wait_ge(x_lo, tile + 1)

            def wait_bank(h, before, m):
                pe.wait_ge(freed_dve if m % 2 else freed_act, h * FREED_HALF + before + m // 2 + 1)

            def group(h, index, tile, count):
                wait_tile(tile)
                for m in range(BANKS):
                    wait_bank(h, EVEN * index, m)
                    mm = three(m, 0, m, True, False)
                mm.then_inc(tile_done, 1)
                with pe.Fori(0, (count - 2) // RING) as i:
                    for s in range(RING):
                        wait_tile(tile + 1 + RING * i + s)
                        for m in range(BANKS):
                            mm = three(m, (1 + s) % RING, m, False, False)
                        mm.then_inc(tile_done, 1)
                wait_tile(tile + count - 1)
                for m in range(BANKS):
                    mm = three(m, 1, m, False, True)
                    mm.then_inc(tile_done if m == BANKS - 1 else bank_done, 1)

            pe.sem_inc(tile_done, RING)
            with pe.Fori(0, HALVES) as h:
                with pe.Fori(0, 4) as n:
                    group(h, n, h * TILES + n * KT, KT)
                with pe.Fori(0, 4) as n:
                    group(h, n + 4, h * TILES + 4 * KT + n * 2 * KT, 2 * KT)
                for m in range(M1 // P):
                    pe.wait_ge(top_in, 16 * h + 32)
                    wait_bank(h, EVEN * GROUPS, m)
                    nc.tensor.matmul(psum[:, m, :], w_dense_sb[:, m * P:(m + 1) * P],
                                     dense_sb[:], start=True, stop=False)
                for k in range(KT):
                    wait_tile(h * TILES + TILES_MID + k)
                    for m in range(M1 // P):
                        mm = three(m, k % RING, m, False, k == KT - 1)
                        if k == KT - 1 and m < M1 // P - 1:
                            mm.then_inc(bank_done, 1)
                    mm.then_inc(tile_done, 1)
                for k in range(TILES_T2):
                    wait_tile(h * TILES + TILES_MID + TILES_T1 + k)
                    for m in range(M2 // P):
                        if k == 0:
                            wait_bank(h, EVEN * GROUPS, 4 + m)
                        mm = three(4 + m, k % RING, m, k == 0, k == TILES_T2 - 1)
                        if k == TILES_T2 - 1 and m < M2 // P - 1:
                            mm.then_inc(bank_done, 1)
                    mm.then_inc(tile_done, 1)
                pe.wait_ge(freed_act, h * FREED_HALF + EVEN * GROUPS + EVEN + 3)
                pe.wait_ge(freed_dve, h * FREED_HALF + EVEN * GROUPS + EVEN + 3)
                for part in range(2):
                    cols = slice(part * HALF // 2, (part + 1) * HALF // 2)
                    for k in range(M2 // P):
                        mm = nc.tensor.matmul(psum[0:1, 6 + part, 0:HALF // 2],
                                              bias[:, W3C + k:W3C + k + 1], acts[:, HID, 4 + k, cols],
                                              start=k == 0, stop=k == M2 // P - 1)
                    mm.then_inc(bank_done, 1)

        @block.scalar
        def _(act):
            act.wait_ge(setup, 1)
            nc.scalar.activation(warm[:], warm[:], ACT.Tanh)
            act.dma_start(w_dense_sb[:], w_dense).then_inc(top_in, 16)
            act.wait_ge(sources_done, 1)
            bases = [nc.scalar.value_load(sel_i[0:1, s:s + 1], min_val=0, max_val=(T0 + 1) * ENTRY)
                     for s in range(2 * NPAIR)]
            act.sem_inc(freed_act, EVEN)

            def split_w(h, tile, width):
                act.wait_ge(w_staged[tile % STAGE], h * (16 * TILES // STAGE) + 16 * (tile // STAGE + 1))
                act.wait_ge(tile_done, h * TILES + tile + 1)
                nc.scalar.activation(w_hl[:, tile % RING, 0, 0:width], w_raw[:, tile % STAGE, 0:width],
                                     ACT.Copy).then_inc(w_hi, 1)

            def split_x(h, tile, g, k):
                wait_source(act, h, g, k)
                act.wait_ge(tile_done, h * TILES + tile + 1)
                scale = scal[:, 0:1] if g == 12 else 1.0
                nc.scalar.activation(x_hl[:, tile % RING, 0, :], x_source(g, k, bases), ACT.Copy if g != 12 else ACT.Identity,
                                     scale=scale).then_inc(x_hi, 1)

            def empty(h, g, m):
                wait_finished(act, h, g, m)
                kind = FINISH[g]
                if kind == "or":
                    act.wait_ge(pair_added, h * KT + m + 1)
                func, entry, b = {"n1": (ACT.Relu, HID, BN1), "n2": (ACT.Tanh, T0 + g // 2, BN2),
                                  "and0": (ACT.Relu, HSUM, BA1), "and1": (ACT.Relu, HID, BA1),
                                  "or": (ACT.Relu, HID, BO1), "z": (ACT.Identity, HSUM, None)}[kind]
                by = bias_z[:, m:m + 1] if b is None else bias[:, b + m:b + m + 1]
                nc.scalar.activation(acts[:, entry, m, :], psum[:, m, :], func, bias=by).then_inc(freed_act, 1)

            def tanh_odd(h, g, m):
                act.wait_ge(freed_dve, h * FREED_HALF + EVEN + EVEN * INDEX[g] + m // 2 + 1)
                tile = acts[:, T0 + g // 2, m, :]
                nc.scalar.activation(tile, tile, ACT.Tanh).then_inc(tanh_done, 1)

            with act.Fori(0, HALVES) as h:
                act.dma_start(dense_sb[:], dense[:, bass.ds(h * HALF, HALF)]).then_inc(top_in, 16)
                for g in range(12):
                    for k in range(KT):
                        tile = g * KT + k
                        split_w(h, tile, H)
                        if k == 0 and g - 1 in FINISH:
                            empty(h, g - 1, 0)
                        split_x(h, tile, g, k)
                        if k == 0 and g - 1 in FINISH:
                            for m in range(2, BANKS, 2):
                                empty(h, g - 1, m)
                            if FINISH[g - 1] == "n2":
                                for m in range(1, BANKS, 2):
                                    tanh_odd(h, g - 1, m)
                split_w(h, TILES_MID, M1)
                for m in range(0, BANKS, 2):
                    empty(h, 11, m)
                for k in range(KT):
                    if k:
                        split_w(h, TILES_MID + k, M1)
                    split_x(h, TILES_MID + k, 12, k)
                first = TILES_MID + TILES_T1
                done = h * DONE_HALF + DONE_TOP
                split_w(h, first, M2)
                for m in range(0, M1 // P, 2):
                    act.wait_ge(bank_done, done + m + 1)
                    nc.scalar.activation(acts[:, HID, m, :], psum[:, m, :], ACT.Relu,
                                         bias=bias[:, BT1 + m:BT1 + m + 1]).then_inc(freed_act, 1)
                for k in range(TILES_T2):
                    if k:
                        split_w(h, first + k, M2)
                    split_x(h, first + k, 13, k)
                act.wait_ge(bank_done, done + 4)
                nc.scalar.activation(acts[:, HID, 4, :], psum[:, 4, :], ACT.Relu,
                                     bias=bias[:, BT2:BT2 + 1]).then_inc(freed_act, 1)
                act.wait_ge(bank_done, done + 5)
                nc.scalar.activation(y_sb[:, 0:HALF // 2], psum[0:1, 6, 0:HALF // 2],
                                     ACT.Copy).then_inc(freed_act, 1)
                act.wait_ge(freed_act, EVEN + (h + 1) * FREED_HALF)
                act.wait_ge(freed_dve, EVEN + (h + 1) * FREED_HALF)
                act.dma_start(out[bass.ds(h * HALF, HALF), :].rearrange("b a -> a b"), y_sb[:]).then_inc(stored, 16)
                act.wait_ge(stored, 16 * (h + 1))

        @block.vector
        def _(dve):
            V = nc.vector
            V.memset(warm[:], 0.0).then_inc(setup, 1)
            dve.sem_inc(w_lo, STAGE)
            dve.sem_inc(turned, GSTAGE)
            dve.sem_inc(freed_dve, EVEN)
            steps = [1]

            def step(ins):
                ins.then_inc(setup, 1)
                steps[0] += 1
                dve.wait_ge(setup, steps[0])

            def over(ap, axis, shape):
                return ap.unsqueeze(axis).to_broadcast(shape)

            dve.wait_ge(consts_in, 64)
            ALL = [P, F, F]
            field = const[:, C_FIELD:C_FIELD + F]
            step(V.tensor_copy(field_f[:], field_i[:]))
            step(V.tensor_copy(row_f, ids_i))
            step(V.tensor_scalar(row_f, row_f, float(Q), None, ALU.mult))
            row3 = row_f.rearrange("p (g f) -> p g f", f=F)
            step(V.tensor_tensor(row3, row3, over(const[:, C_BASE:C_BASE + F], 1, [P, HALVES * GATHERS, F]),
                                 ALU.add))
            step(V.tensor_tensor(onehot[:, 0:SLOTS, :], over(field_f[:], 2, ALL), over(field, 1, ALL),
                                 ALU.is_equal))

            def index_column(s):
                step(V.tensor_tensor(picked[:], row3, over(onehot[:, s, :], 1, [P, HALVES * GATHERS, F]),
                                     ALU.mult))
                with nc.allow_low_precision(reason="one non-zero integer below 2^24 in each sum"):
                    V.tensor_reduce(idx[:, :, s, :], picked[:].rearrange("p (h g) f -> p h g f", h=HALVES),
                                    AX.X, ALU.add).then_inc(idx_done, 1)
                dve.wait_ge(idx_done, s + 1)

            index_column(N0)
            is_not, in_pair, rest, rest_rows, so_far = (mask[:, i, :] for i in range(5))
            is0, is1, both, to = (same[:, i, :] for i in range(4))
            sides = 2 * NPAIR
            step(V.tensor_scalar(is0, field_f[:, 2:SLOTS], field_f[:, N0:N0 + 1], None, ALU.is_equal))
            step(V.tensor_scalar(is1, field_f[:, 2:SLOTS], field_f[:, N1:N1 + 1], None, ALU.is_equal))
            step(V.tensor_tensor(both, is0, is1, ALU.mult))
            step(V.tensor_tensor(is1, is1, both, ALU.subtract))
            step(V.tensor_tensor(is1, is1, const[:, C_TO1:C_TO1 + sides], ALU.mult))
            step(V.tensor_tensor(is0, is0, const[:, C_TO0:C_TO0 + sides], ALU.mult))
            step(V.tensor_tensor(to, is0, is1, ALU.add))
            step(V.tensor_tensor(sel_f[:, 0:sides], to, const[:, C_OWN:C_OWN + sides], ALU.add))
            V.tensor_copy(sel_i[:, 0:sides], sel_f[:, 0:sides]).then_inc(sources_done, 1)
            index_column(N1)
            step(V.tensor_tensor(is_not, onehot[:, N0, :], onehot[:, N1, :], ALU.max))
            step(V.tensor_reduce(in_pair, onehot[:, A00:SLOTS, :].rearrange("p s f -> p f s"), AX.X, ALU.max))
            step(V.tensor_scalar(rest, in_pair, -1.0, 1.0, ALU.mult, ALU.add))
            step(V.tensor_scalar(rest_rows, is_not, -1.0, 1.0, ALU.mult, ALU.add))
            step(V.tensor_tensor(rest_rows, rest_rows, rest, ALU.mult))
            step(V.tensor_reduce(scal[:, 1:2], rest, AX.X, ALU.add))
            step(V.tensor_scalar(scal[:, 1:2], scal[:, 1:2], float(NPAIR), None, ALU.add))
            step(V.reciprocal(scal[:, 0:1], scal[:, 1:2]))
            step(V.tensor_tensor(square[:, 0:2, :], onehot[:, N0:N1 + 1, :], over(rest, 1, [P, 2, F]), ALU.mult))
            step(V.tensor_reduce(scal[:, 2:4], square[:, 0:2, :], AX.X, ALU.add))
            step(V.tensor_tensor(scal[:, 4:5], field_f[:, N0:N0 + 1], field_f[:, N1:N1 + 1], ALU.not_equal))
            step(V.tensor_tensor(scal[:, 3:4], scal[:, 3:4], scal[:, 4:5], ALU.mult))
            upto = const[:, C_UPTO:C_UPTO + F * F].rearrange("p (f g) -> p f g", g=F)
            step(V.tensor_tensor(square[:], upto, over(rest_rows, 1, ALL), ALU.mult))
            step(V.tensor_reduce(so_far, square[:], AX.X, ALU.add))
            picks = onehot[:, REST:REST + F, :]
            step(V.tensor_tensor(picks, over(so_far, 1, ALL), over(const[:, C_RANK:C_RANK + F], 2, ALL),
                                 ALU.is_equal))
            step(V.tensor_tensor(picks, picks, over(rest_rows, 1, ALL), ALU.mult))
            step(V.tensor_reduce(left_over[:], picks, AX.X, ALU.add))
            step(V.tensor_copy(sel_i[:, sides:sides + 1], so_far[:, F - 1:F]))
            step(V.scalar_tensor_tensor(out=bias_z[:], in0=bias[:, BA2:BA2 + KT], scalar=2.0,
                                        in1=bias[:, BO2:BO2 + KT], op0=ALU.mult, op1=ALU.add))
            dve.wait_ge(sources_done, 1)
            bases = [V.value_load(sel_i[0:1, s:s + 1], min_val=0, max_val=(T0 + 1) * ENTRY)
                     for s in range(sides)]
            more = V.value_load(sel_i[0:1, sides:sides + 1], min_val=0, max_val=F)

            def split_w(h, tile, width):
                dve.wait_ge(w_hi, h * TILES + tile + 1)
                V.tensor_tensor(w_hl[:, tile % RING, 1, 0:width], w_raw[:, tile % STAGE, 0:width],
                                w_hl[:, tile % RING, 0, 0:width], ALU.subtract).then_inc(w_lo, 1)

            def split_x(h, tile, g, k):
                wait_source(dve, h, g, k)
                dve.wait_ge(x_hi, h * TILES + tile + 1)
                hi, lo = x_hl[:, tile % RING, 0, :], x_hl[:, tile % RING, 1, :]
                if g == 12:
                    ins = V.scalar_tensor_tensor(out=lo, in0=x_source(g, k, bases), scalar=scal[:, 0:1],
                                                 in1=hi, op0=ALU.mult, op1=ALU.subtract)
                else:
                    ins = V.tensor_tensor(lo, x_source(g, k, bases), hi, ALU.subtract)
                ins.then_inc(x_lo, 1)

            def empty(h, g, m):
                wait_finished(dve, h, g, m)
                kind = FINISH[g]
                entry, b = {"n1": (HID, BN1), "n2": (T0 + g // 2, BN2), "and0": (HSUM, BA1),
                            "and1": (HID, BA1), "or": (HID, BO1), "z": (HSUM, None)}[kind]
                by = bias_z[:, m:m + 1] if b is None else bias[:, b + m:b + m + 1]
                if kind == "or":
                    dve.wait_ge(pair_added, h * KT + m + 1)
                if kind in ("n2", "z"):
                    ins = V.tensor_scalar(acts[:, entry, m, :], psum[:, m, :], by, None, ALU.add)
                else:
                    ins = V.tensor_scalar(acts[:, entry, m, :], psum[:, m, :], by, 0.0, ALU.add, ALU.max)
                ins.then_inc(freed_dve, 1)

            def turn(h, unit, entry, g):
                dve.wait_ge(gathered[unit % GSTAGE],
                            h * (16 * UNITS_HALF // GSTAGE) + 16 * (unit // GSTAGE + 1))
                V.transpose(acts[:, entry, :, g * LANE:(g + 1) * LANE],
                            rows[:, unit % GSTAGE, :].rearrange("p (b f) -> p b f", f=LANE)).then_inc(turned, 1)

            def sum_rest(h, unit, g):
                now = h * UNITS_HALF + GSTAGE + unit
                for r in range(2):
                    dve.wait_ge(gathered[(unit + r) % GSTAGE],
                                h * (16 * UNITS_HALF // GSTAGE) + 16 * ((unit + r) // GSTAGE + 1))
                if g:
                    dve.wait_ge(rest_turned, h * GATHERS + g)
                V.tensor_scalar(rest_sum[:], rows[:, unit % GSTAGE, :], left_over[:, 0:1], None,
                                ALU.mult).then_inc(turned, 1)
                dve.wait_ge(turned, now + 1)
                V.scalar_tensor_tensor(out=rest_sum[:], in0=rows[:, (unit + 1) % GSTAGE, :],
                                       scalar=left_over[:, 1:2], in1=rest_sum[:], op0=ALU.mult,
                                       op1=ALU.add).then_inc(turned, 1)
                dve.wait_ge(turned, now + 2)
                V.transpose(acts[:, Z, :, g * LANE:(g + 1) * LANE],
                            rest_sum[:].rearrange("p (b f) -> p b f", f=LANE)).then_inc(rest_turned, 1)

            def add_more(h):
                extra = F - 2
                with dve.Fori(0, GATHERS) as g:
                    done = (h * GATHERS + g) * (extra + 2)
                    for r in range(extra):
                        n = (h * GATHERS + g) * extra + r
                        column = idx[:, bass.ds(h, 1), REST + 2 + r, bass.ds(g, 1)].rearrange("p a b -> p (a b)")
                        V.tensor_copy(more_idx[:], column).then_inc(more_asked, 1)
                        dve.wait_ge(more_got, 16 * n + 16)
                        c = left_over[:, 2 + r:3 + r]
                        if r == 0:
                            V.tensor_scalar(rest_sum[:], more_rows[:], c, None, ALU.mult).then_inc(more_step, 1)
                        else:
                            V.scalar_tensor_tensor(out=rest_sum[:], in0=more_rows[:], scalar=c, in1=rest_sum[:],
                                                   op0=ALU.mult, op1=ALU.add).then_inc(more_step, 1)
                        dve.wait_ge(more_step, done + r + 1)
                    V.transpose(more_turned[:], rest_sum[:].rearrange("p (b f) -> p b f", f=LANE)
                                ).then_inc(more_step, 1)
                    dve.wait_ge(more_step, done + extra + 1)
                    dve.wait_ge(rest_turned, (h + 1) * GATHERS)
                    z = acts[:, Z, :, bass.ds(g * LANE, LANE)]
                    V.tensor_tensor(z, z, more_turned[:], ALU.add).then_inc(more_step, 1)
                    dve.wait_ge(more_step, done + extra + 2)

            def add_not(h, n, k):
                dve.wait_ge(tanh_done, h * KT + EVEN * (n + 1))
                if n:
                    dve.wait_ge(z_added, h * 2 * KT + k + 1)
                z = acts[:, Z, k, :]
                V.scalar_tensor_tensor(out=z, in0=acts[:, T0 + n, k, :], scalar=scal[:, 2 + n:3 + n], in1=z,
                                       op0=ALU.mult, op1=ALU.add).then_inc(z_added, 1)

            def add_pair(h, m):
                dve.wait_ge(freed_dve if m % 2 else freed_act,
                            h * FREED_HALF + EVEN + EVEN * INDEX[7] + m // 2 + 1)
                V.tensor_tensor(acts[:, HSUM, m, :], acts[:, HSUM, m, :], acts[:, HID, m, :],
                                ALU.add).then_inc(pair_added, 1)

            def add_z(h, m):
                dve.wait_ge(freed_dve if m % 2 else freed_act,
                            h * FREED_HALF + EVEN + EVEN * INDEX[11] + m // 2 + 1)
                V.tensor_tensor(acts[:, Z, m, :], acts[:, Z, m, :], acts[:, HSUM, m, :],
                                ALU.add).then_inc(z_ready, 1)

            for g in range(GATHERS):
                turn(0, g, ENTRY_OF[N0], g)
                if g + 2 < SLOTS + F:
                    index_column(g + 2)

            BESIDES = {0: N1, 1: A00, 2: A01, 3: A10, 4: REST_JOB, 5: REST_JOB, 6: A11, 7: O0, 8: O1, 9: N0}

            def besides(h, g, k):
                def share(n, tiles=range(1, KT - 1)):
                    per = -(-n // len(tiles))
                    i = k - tiles[0]
                    return range(i * per, min(n, (i + 1) * per)) if k in tiles else ()

                job = BESIDES.get(g)
                if job == REST_JOB:
                    half = GATHERS // 2
                    for i in share(half, range(1, KT)):
                        c = i + half * (g == 5)
                        sum_rest(h, FIRST_UNIT[job] + 2 * c, c)
                    if g == 5 and k == KT - 1:
                        with dve.If(more > 2):
                            add_more(h)
                elif job == N0:
                    if len(share(GATHERS)):
                        with dve.If(h < HALVES - 1):
                            for c in share(GATHERS):
                                turn(h, FIRST_UNIT[job] + c, ENTRY_OF[job], c)
                elif job is not None:
                    for c in share(GATHERS):
                        turn(h, FIRST_UNIT[job] + c, ENTRY_OF[job], c)
                if g == 8 and k:
                    add_pair(h, k - 1)
                    if k == KT - 1:
                        add_pair(h, k)
                if g == 10:
                    if k == 1:
                        dve.wait_ge(rest_turned, (h + 1) * GATHERS)
                    for i in share(2 * KT):
                        add_not(h, i // KT, i % KT)

            with dve.Fori(0, HALVES) as h:
                for g in range(12):
                    for k in range(KT):
                        tile = g * KT + k
                        split_w(h, tile, H)
                        split_x(h, tile, g, k)
                        if k == 0 and g - 1 in FINISH:
                            for m in range(1, BANKS, 2):
                                empty(h, g - 1, m)
                        besides(h, g, k)
                split_w(h, TILES_MID, M1)
                dve.wait_ge(z_added, (h + 1) * 2 * KT)
                for m in range(KT):
                    if m % 2:
                        empty(h, 11, m)
                    add_z(h, m)
                    if m == 0:
                        split_x(h, TILES_MID, 12, 0)
                for k in range(1, KT):
                    split_w(h, TILES_MID + k, M1)
                    split_x(h, TILES_MID + k, 12, k)
                first = TILES_MID + TILES_T1
                done = h * DONE_HALF + DONE_TOP
                split_w(h, first, M2)
                for m in range(1, M1 // P, 2):
                    if m < M1 // P - 1:
                        dve.wait_ge(bank_done, done + m + 1)
                    else:
                        dve.wait_ge(tile_done, h * TILES + RING + first)
                    V.tensor_scalar(acts[:, HID, m, :], psum[:, m, :], bias[:, BT1 + m:BT1 + m + 1], 0.0,
                                    ALU.add, ALU.max).then_inc(freed_dve, 1)
                for k in range(TILES_T2):
                    if k:
                        split_w(h, first + k, M2)
                    split_x(h, first + k, 13, k)
                dve.wait_ge(tile_done, h * TILES + RING + TILES)
                V.tensor_scalar(acts[:, HID, 5, :], psum[:, 5, :], bias[:, BT2 + 1:BT2 + 2], 0.0,
                                ALU.add, ALU.max).then_inc(freed_dve, 1)
                dve.wait_ge(bank_done, done + 6)
                V.tensor_copy(y_sb[:, HALF // 2:HALF],
                              psum[0:1, 7, 0:HALF // 2]).then_inc(freed_dve, 1)


def feature_rows(w):
    k, n = w.shape
    return w.reshape(k // H, Q, KT, LANE, n).transpose(0, 2, 1, 3, 4).reshape(k // P, P, n)


def feature_columns(w):
    k = w.shape[0]
    return w.reshape(k, Q, KT, LANE).transpose(0, 2, 1, 3).reshape(k, H)


def plain_rows(w):
    return w.reshape(-1, P, w.shape[1])


def bias_columns(b):
    return b.reshape(-1, P).T


def feature_bias(b):
    return bias_columns(feature_columns(b.reshape(1, H)).reshape(H))


def constants():
    quadrant = np.arange(P)[:, None] // LANE
    first_row = np.concatenate([[0], np.cumsum(VOCAB)[:-1]])[None, :]
    own = np.array([ENTRY_OF[slot] * ENTRY for slot in range(2, SLOTS)] + [0] * (F - 2 * NPAIR))
    every = [np.arange(F), None, np.arange(F) + 1, own, T0 * ENTRY - own, (T0 + 1) * ENTRY - own,
             np.tril(np.ones((F, F))).reshape(-1)]
    return np.concatenate([Q * first_row + quadrant if c is None else np.tile(c, (P, 1)) for c in every],
                          axis=1).astype(np.float32)


def kernel(**inputs):
    import concourse.bacc as bacc
    from concourse.bass_utils import run_bass_kernel_spmd

    x = {name: np.asarray(value) for name, value in inputs.items()}
    n1, n2, a1, a2, o1, o2 = (x["L0_rec_W" + n] for n in ("n1", "n2", "a1", "a2", "o1", "o2"))
    field_rows = np.concatenate([x["L0_rec_not_idx"], x["L0_rec_and_pairs"].reshape(-1),
                                 x["L0_rec_or_pairs"].reshape(-1)])
    arrays = {
        "table": np.concatenate([x[f"tbl_{f}"] for f in range(F)]).reshape(-1, QUARTER),
        "ids": np.tile(x["ids"].reshape(HALVES * GATHERS, LANE, F).transpose(1, 0, 2).reshape(LANE, -1), (Q, 1)),
        "fields": np.tile(field_rows.reshape(1, F), (P, 1)),
        "consts": constants(),
        "biases": np.concatenate([
            bias_columns(x["L0_rec_bn1"]), feature_bias(x["L0_rec_bn2"]), bias_columns(x["L0_rec_ba1"]),
            feature_bias(x["L0_rec_ba2"]), bias_columns(x["L0_rec_bo1"]), feature_bias(x["L0_rec_bo2"]),
            bias_columns(x["b_top1"]), bias_columns(x["b_top2"]), bias_columns(x["W_top3"])], axis=1),
        "w_mid": np.concatenate([
            feature_rows(n1), plain_rows(feature_columns(n2)), feature_rows(a1), feature_rows(o1),
            plain_rows(feature_columns(a2)), plain_rows(feature_columns(o2))]),
        "w_t1": feature_rows(x["W_top1"][:H]),
        "w_t2": plain_rows(x["W_top2"]),
        "w_dense": x["W_top1"][H:],
        "dense": x["dense_ctx"].T,
    }
    arrays = {name: np.ascontiguousarray(a) for name, a in arrays.items()}
    nc = bacc.Bacc("TRN2", target_bir_lowering=False, num_devices=1)
    args = [nc.dram_tensor(f"in_{name}", a.shape, mybir.dt.from_np(a.dtype), kind="ExternalInput").ap()
            for name, a in arrays.items()]
    out = nc.dram_tensor("y", (B, 1), F32, kind="ExternalOutput").ap()
    build_tower(nc, *args, out)
    result = run_bass_kernel_spmd(nc, [{f"in_{name}": a for name, a in arrays.items()}], core_ids=[0])
    return result.results[0]["y"]
```
